# Optimizing a Trainium2 kernel written in Bass

```python
import numpy as np
import jax
import jax.numpy as jnp

def _softmax(x, axis=-1):
    return jax.nn.softmax(x, axis=axis)

def _gelu(x):
    return jax.nn.gelu(x, approximate=True)

def _silu(x):
    return jax.nn.silu(x)

def _sigmoid(x):
    return jax.nn.sigmoid(x)

def _layernorm(x, axis=-1, eps=1e-05):
    m = jnp.mean(x, axis=axis, keepdims=True)
    v = jnp.var(x, axis=axis, keepdims=True)
    return (x - m) / jnp.sqrt(v + eps)

def _scatter_add(tgt, idx, src, axis=0):
    return tgt.at[idx].add(src)

def _segment_sum(src, seg, n):
    return jax.ops.segment_sum(src, seg, n)
kernel_name = 'mk_cond_resid_d1_seqx_r4_83507a'

def setup_inputs(seed: int=0):
    np.random.seed(seed)
    _w = jnp.asarray

    def _rec_inputs():
        import jax
        import jax.numpy as jnp
        _rk = jax.random.key(seed)
        x = -1.394e-06 + 0.9999 * jax.random.normal(jax.random.fold_in(_rk, 1), (128, 64, 512), jnp.float32)
        _lenS = 64 - jax.random.randint(jax.random.fold_in(_rk, 7), (128,), 0, max(1, 64 // 4) + 1, jnp.int32)
        _lenS2 = 64 - jax.random.randint(jax.random.fold_in(_rk, 8), (128,), 0, max(1, 64 // 4) + 1, jnp.int32)
        cond_2048 = -0.00499425 + 1.0058 * jax.random.normal(jax.random.fold_in(_rk, 11), (128, 512), jnp.float32)
        return (x, cond_2048)
    x, cond_2048 = _rec_inputs()

    def _L0_cond_setup():
        import jax, jax.numpy as jnp
        import numpy as np
        B, T, D = (16, 128, 512)
        key = jax.random.key(seed)
        k0, k1, k2, k3 = jax.random.split(key, 4)
        scale = 1.0 / np.sqrt(D)
        return {'initial_state': jax.random.normal(k0, (B, D), jnp.float32), 'inputs': jax.random.normal(k1, (B, T, D), jnp.float32), 'W_ih': jax.random.normal(k2, (D, 3 * D), jnp.float32) * scale, 'W_hh': jax.random.normal(k3, (D, 3 * D), jnp.float32) * scale, 'b_ih': jnp.zeros((3 * D,), jnp.float32), 'b_hh': jnp.zeros((3 * D,), jnp.float32)}
    _L0_cond_all = _L0_cond_setup()
    _L0_cond_in = {k: v for k, v in _L0_cond_all.items() if k in ('W_ih', 'W_hh', 'b_ih', 'b_hh')}
    del _L0_cond_all
    return {'x': x, 'cond_2048': cond_2048, 'L0_cond_W_ih': _L0_cond_in['W_ih'], 'L0_cond_W_hh': _L0_cond_in['W_hh'], 'L0_cond_b_ih': _L0_cond_in['b_ih'], 'L0_cond_b_hh': _L0_cond_in['b_hh']}

def reference(x, cond_2048, L0_cond_W_ih, L0_cond_W_hh, L0_cond_b_ih, L0_cond_b_hh):
    import jax
    import jax.numpy as jnp

    def _L0_cond_ref(initial_state, inputs, W_ih, W_hh, b_ih, b_hh):
        import jax, jax.numpy as jnp
        import numpy as np
        B, T, D = (16, 128, 512)
        "ScanOverTime(GRU cell): sequential per-timestep module call with\n            dict-state passing; merge_dict_trees stacks the per-step\n            'state_predicted' tensors along axis=1 -> [B, T, D]."

        def cell(h, x):
            gi = x @ W_ih + b_ih
            gh = h @ W_hh + b_hh
            i_r, i_z, i_n = jnp.split(gi, 3, axis=-1)
            h_r, h_z, h_n = jnp.split(gh, 3, axis=-1)
            r = jax.nn.sigmoid(i_r + h_r)
            z = jax.nn.sigmoid(i_z + h_z)
            n = jnp.tanh(i_n + r * h_n)
            h_new = (1.0 - z) * n + z * h
            return (h_new, h_new)
        xs = jnp.swapaxes(inputs, 0, 1)
        _, hs = jax.lax.scan(cell, initial_state, xs)
        return jnp.swapaxes(hs, 0, 1)
    x = x + _L0_cond_ref(cond_2048, x, L0_cond_W_ih, L0_cond_W_hh, L0_cond_b_ih, L0_cond_b_hh)
    return x

_drawn_inputs = setup_inputs


def setup_inputs(seed=0):
    import zlib

    import numpy as np

    out = dict(_drawn_inputs(seed))
    spreads = {'L0_cond_b_ih': (0.0, 0.1), 'L0_cond_b_hh': (0.0, 0.1)}
    factors = {}
    for name, (base, spread) in spreads.items():
        noise = np.random.default_rng([zlib.crc32(name.encode()), seed]).standard_normal(out[name].shape)
        drawn = base * np.exp(spread * noise) if base else spread * noise
        out[name] = jnp.asarray(drawn.astype(out[name].dtype))
    for name, factor in factors.items():
        out[name] = (out[name] * factor).astype(out[name].dtype)
    return out
```

```python
from contextlib import ExitStack

import concourse.bass as bass
from concourse import mybir

P = 128
UNROLL = 4
GATE_R, GATE_Z, GATE_N = range(3)
LOAD_ORDER = (GATE_R, GATE_Z, GATE_N)
STATE_ORDER = (GATE_R, GATE_N, GATE_Z)


def build(nc, x_t, cond, w_ih, w_hh, b_ih, b_hh, out_t):
    f32 = mybir.dt.float32
    f32r = mybir.dt.float32r
    ALU = mybir.AluOpType
    ACT = mybir.ActivationFunctionType

    T = x_t.shape[0]
    D = cond.shape[1]
    C = D // P
    G = w_ih.shape[1] // D
    HALF = D // 2
    HC = C // 2
    TURNS = T // UNROLL
    LAST_BLOCK = T - UNROLL
    assert T % UNROLL == 0 and TURNS >= 3 and cond.shape[0] == P

    with ExitStack() as ctx:
        def sb(name, shape, dt=f32):
            return ctx.enter_context(nc.sbuf_tensor(name, shape, dt))

        def bank(name):
            return ctx.enter_context(nc.psum_tensor(name, [P, D], f32))

        def sem(name):
            return ctx.enter_context(nc.semaphore(name))

        wi_raw = sb("wi_raw", [P, G, C, D])
        wi_hi = sb("wi_hi", [P, G, C, D], f32r)
        wi_lo = sb("wi_lo", [P, G, C, D], f32r)
        wh_raw = sb("wh_raw", [P, G, C, D])
        wh_hi = sb("wh_hi", [P, G, C, D], f32r)
        wh_lo = sb("wh_lo", [P, G, C, D], f32r)
        bi = sb("bi", [P, G * D])
        bh = sb("bh", [P, G * D])
        identity = sb("identity", [P, P])
        x_raw = [sb(f"x_raw{s}", [P, D]) for s in range(UNROLL)]
        x_hi = [sb(f"x_hi{s}", [P, D], f32r) for s in range(2)]
        x_lo = [sb(f"x_lo{s}", [P, D], f32r) for s in range(2)]
        h = [sb(f"h{s}", [P, D]) for s in range(2)]
        hT_hi = sb("hT_hi", [P, D], f32r)
        hT_lo = sb("hT_lo", [P, D], f32r)
        gin = sb("gin", [P, D])
        ghn = sb("ghn", [P, D])
        pre_r = sb("pre_r", [P, D])
        pre_z = sb("pre_z", [P, D])
        r_gate = sb("r_gate", [P, D])
        z_gate = sb("z_gate", [P, D])
        r_ghn = sb("r_ghn", [P, D])
        pre_n = sb("pre_n", [P, D])
        n_gate = sb("n_gate", [P, D])
        h_less_n = sb("h_less_n", [P, D])
        z_part = sb("z_part", [P, D])
        out_sb = [sb(f"out_sb{s}", [P, D]) for s in range(2)]

        ps_r = [bank(f"ps_r{s}") for s in range(2)]
        ps_z = [bank(f"ps_z{s}") for s in range(2)]
        ps_in = bank("ps_in")
        ps_hn = bank("ps_hn")
        ps_hT = ctx.enter_context(nc.psum_tensor("ps_hT", [P, 2, D], f32))

        wi_loaded = [[sem(f"wi_loaded{g}{k}") for k in range(2)] for g in range(G)]
        wh_loaded = [[sem(f"wh_loaded{g}{k}") for k in range(2)] for g in range(G)]
        bias_loaded = sem("bias_loaded")
        cond_loaded = sem("cond_loaded")
        x_loaded = [sem(f"x_loaded{s}") for s in range(UNROLL)]
        out_stored = [sem(f"out_stored{s}") for s in range(2)]
        identity_zeroed = sem("identity_zeroed")
        identity_ready = sem("identity_ready")
        bias_ready = sem("bias_ready")
        w_hi_ready = sem("w_hi_ready")
        w_lo_ready = sem("w_lo_ready")
        x_hi_ready = sem("x_hi_ready")
        x_lo_ready = sem("x_lo_ready")
        in_sum_ready = sem("in_sum_ready")
        r_sum_ready = sem("r_sum_ready")
        hn_sum_ready = sem("hn_sum_ready")
        z_sum_ready = sem("z_sum_ready")
        gin_ready = sem("gin_ready")
        pre_r_ready = sem("pre_r_ready")
        r_ready = sem("r_ready")
        ghn_ready = sem("ghn_ready")
        r_ghn_ready = sem("r_ghn_ready")
        pre_n_ready = sem("pre_n_ready")
        n_ready = sem("n_ready")
        pre_z_ready = sem("pre_z_ready")
        z_ready = sem("z_ready")
        h_less_n_ready = sem("h_less_n_ready")
        z_part_ready = sem("z_part_ready")
        h_ready = sem("h_ready")
        hT_ready = [sem(f"hT_ready{k}") for k in range(2)]
        hT_hi_ready = [sem(f"hT_hi_ready{k}") for k in range(2)]
        hT_lo_ready = [sem(f"hT_lo_ready{k}") for k in range(2)]
        out_ready = sem("out_ready")

        halves = [slice(0, HALF), slice(HALF, D)]
        pieces = [(wi_raw, wi_hi, wi_lo, wi_loaded, w_ih, g, k) for g in LOAD_ORDER for k in range(2)]
        pieces += [(wh_raw, wh_hi, wh_lo, wh_loaded, w_hh, g, k) for g in STATE_ORDER for k in range(2)]
        w_pieces = {(w is w_hh, g, k): n + 1 for n, (_, _, _, _, w, g, k) in enumerate(pieces)}

        block = ctx.enter_context(nc.Block())

        @block.sync
        def _(sp):
            def load_x(t, u):
                sp.dma_start(x_raw[u][:, :], x_t[bass.ds(t, 1), :, :].rearrange("a p n -> p (a n)")
                             ).then_inc(x_loaded[u], 16)

            def load_piece(raw, hi, lo, loaded, w, g, k):
                rows = w[k * HC * P:(k + 1) * HC * P, g * D:(g + 1) * D]
                sp.dma_start(raw[:, g, k * HC:(k + 1) * HC, :],
                             rows.rearrange("(c p) n -> p c n", p=P)).then_inc(loaded[g][k], 16)

            load_x(0, 0)
            for piece in pieces[:G * 2]:
                load_piece(*piece)
            load_x(1, 1)
            for piece in pieces[G * 2:]:
                load_piece(*piece)
            for u in range(2, UNROLL):
                load_x(u, u)

            def step(t, u, more):
                sp.wait_ge(out_ready, t + 1)
                sp.dma_start(out_t[bass.ds(t, 1), :, :].rearrange("a p n -> p (a n)"), out_sb[u % 2][:, :]
                             ).then_inc(out_stored[u % 2], 16)
                if more:
                    load_x(t + UNROLL, u)

            for u in range(UNROLL):
                step(u, u, True)
            with sp.Fori(1, TURNS - 1) as turn:
                for u in range(UNROLL):
                    step(turn * UNROLL + u, u, True)
            for u in range(UNROLL):
                step(LAST_BLOCK + u, u, False)
            for s in range(2):
                sp.wait_ge(out_stored[s], 16 * (T // 2))

        @block.tensor
        def _(pe):
            def products(out, a_hi, a_lo, w_hi, w_lo, g, c, first, last):
                rows = slice(c * P, (c + 1) * P)
                nc.tensor.matmul(out[:, :], a_hi[:, rows], w_hi[:, g, c, :], start=first, stop=False)
                nc.tensor.matmul(out[:, :], a_hi[:, rows], w_lo[:, g, c, :], start=False, stop=False)
                return nc.tensor.matmul(out[:, :], a_lo[:, rows], w_hi[:, g, c, :], start=False, stop=last)

            def input_products(g, out, s, first_step):
                for c in range(C):
                    if first_step and c % HC == 0:
                        pe.wait_ge(w_lo_ready, w_pieces[False, g, c // HC])
                    last = products(out, x_hi[s], x_lo[s], wi_hi, wi_lo, g, c, c == 0, g == GATE_N and c == C - 1)
                return last

            def state_products(g, out, first_step):
                for c in range(C):
                    if first_step and c % HC == 0:
                        pe.wait_ge(w_lo_ready, w_pieces[True, g, c // HC])
                    last = products(out, hT_hi, hT_lo, wh_hi, wh_lo, g, c, g == GATE_N and c == 0, c == C - 1)
                return last

            def transpose_state(s):
                for k in range(2):
                    for c in range(HC):
                        rows = slice((k * HC + c) * P, (k * HC + c + 1) * P)
                        last = nc.tensor.transpose(ps_hT[:, k, c * P:(c + 1) * P], h[s][:, rows], identity[:, :])
                    last.then_inc(hT_ready[k], 1)

            pe.wait_ge(x_hi_ready, 1)
            pe.wait_ge(x_lo_ready, 1)
            input_products(GATE_R, ps_r[0], 0, True)
            input_products(GATE_Z, ps_z[0], 0, True)
            pe.wait_ge(identity_ready, 1)
            pe.wait_ge(cond_loaded, 16)
            transpose_state(1)
            last = input_products(GATE_N, ps_in, 0, True)
            last.then_inc(in_sum_ready, 1)

            def step(t, u, first_step=False, more=True):
                s, nxt = u % 2, (u + 1) % 2
                for n, g in enumerate(STATE_ORDER):
                    if n == 0:
                        pe.wait_ge(hT_lo_ready[0], t + 1)
                        pe.wait_ge(hT_lo_ready[1], t + 1)
                    if g == GATE_N and not first_step:
                        pe.wait_ge(ghn_ready, t)
                    out, ready = {GATE_R: (ps_r[s], r_sum_ready), GATE_Z: (ps_z[s], z_sum_ready),
                                  GATE_N: (ps_hn, hn_sum_ready)}[g]
                    state_products(g, out, first_step).then_inc(ready, 1)
                if more:
                    pe.wait_ge(x_hi_ready, t + 2)
                    pe.wait_ge(x_lo_ready, t + 2)
                    if not first_step:
                        pe.wait_ge(pre_r_ready, t)
                        pe.wait_ge(pre_z_ready, t)
                    input_products(GATE_R, ps_r[nxt], nxt, False)
                    input_products(GATE_Z, ps_z[nxt], nxt, False)
                pe.wait_ge(h_ready, t + 1)
                if not first_step:
                    pe.wait_ge(out_ready, t)
                transpose_state(s)
                if more:
                    pe.wait_ge(gin_ready, t + 1)
                    input_products(GATE_N, ps_in, nxt, False).then_inc(in_sum_ready, 1)

            for u in range(UNROLL):
                step(u, u, first_step=u == 0)
            with pe.Fori(1, TURNS - 1) as turn:
                for u in range(UNROLL):
                    step(turn * UNROLL + u, u)
            for u in range(UNROLL):
                step(LAST_BLOCK + u, u, more=u < UNROLL - 1)

        @block.scalar
        def _(act):
            act.dma_start(h[1][:, :], cond[:, :]).then_inc(cond_loaded, 16)
            act.dma_start(bi[:, :], b_ih.rearrange("(a n) -> a n", a=1).to_broadcast([P, G * D])).then_inc(bias_loaded, 16)
            act.dma_start(bh[:, :], b_hh.rearrange("(a n) -> a n", a=1).to_broadcast([P, G * D])).then_inc(bias_loaded, 16)

            def round_x(block_start, v):
                act.wait_ge(x_loaded[v], block_start * (16 // UNROLL) + 16)
                nc.scalar.activation(x_hi[v % 2][:, :], x_raw[v][:, :], ACT.Copy).then_inc(x_hi_ready, 1)

            def round_state(count):
                for k in range(2):
                    act.wait_ge(hT_ready[k], count)
                    nc.scalar.activation(hT_hi[:, halves[k]], ps_hT[:, k, 0:HALF], ACT.Copy
                                         ).then_inc(hT_hi_ready[k], 1)

            def round_piece(raw, hi, lo, loaded, w, g, k):
                act.wait_ge(loaded[g][k], 16)
                chunks = slice(k * HC, (k + 1) * HC)
                nc.scalar.activation(hi[:, g, chunks, :], raw[:, g, chunks, :], ACT.Copy).then_inc(w_hi_ready, 1)

            round_x(0, 0)
            for piece in pieces[:G * 2]:
                round_piece(*piece)
            round_x(0, 1)
            round_state(1)
            for piece in pieces[G * 2:]:
                round_piece(*piece)

            def step(base, u, more_x=True, more=True):
                t = base + u
                if more_x:
                    act.wait_ge(in_sum_ready, t + 1)
                    ahead = (u + 2) // UNROLL * UNROLL
                    round_x(base + ahead, u + 2 - ahead)
                act.wait_ge(pre_r_ready, t + 1)
                nc.scalar.activation(r_gate[:, :], pre_r[:, :], ACT.Sigmoid).then_inc(r_ready, 1)
                act.wait_ge(pre_n_ready, t + 1)
                nc.scalar.activation(n_gate[:, :], pre_n[:, :], ACT.Tanh).then_inc(n_ready, 1)
                act.wait_ge(pre_z_ready, t + 1)
                nc.scalar.activation(z_gate[:, :], pre_z[:, :], ACT.Sigmoid).then_inc(z_ready, 1)
                if more:
                    round_state(t + 2)

            for u in range(UNROLL):
                step(0, u)
            with act.Fori(1, TURNS - 1) as turn:
                for u in range(UNROLL):
                    step(turn * UNROLL, u)
            for u in range(UNROLL):
                step(LAST_BLOCK, u, more_x=u + 2 < UNROLL, more=u + 1 < UNROLL)

        @block.gpsimd
        def _(pool):
            nc.gpsimd.memset(identity[:, :], 0.0).then_inc(identity_zeroed, 1)
            pool.wait_ge(identity_zeroed, 1)
            nc.gpsimd.affine_select(out=identity[:, :], in_=identity[:, :], compare_op=ALU.not_equal, fill=1.0,
                                    base=0, pattern=[[-1, P]], channel_multiplier=1).then_inc(identity_ready, 1)

            def split_x(t, v):
                pool.wait_ge(x_hi_ready, t + 1)
                nc.gpsimd.tensor_tensor(x_lo[v % 2][:, :], x_raw[v][:, :], x_hi[v % 2][:, :].bitcast(f32),
                                        ALU.subtract).then_inc(x_lo_ready, 1)

            for v in range(UNROLL):
                split_x(v, v)
            with pool.Fori(1, TURNS) as turn:
                for v in range(UNROLL):
                    split_x(turn * UNROLL + v, v)

        @block.vector
        def _(dve):
            def split_piece(n, raw, hi, lo, loaded, w, g, k):
                dve.wait_ge(w_hi_ready, n + 1)
                chunks = slice(k * HC, (k + 1) * HC)
                nc.vector.tensor_tensor(lo[:, g, chunks, :], raw[:, g, chunks, :], hi[:, g, chunks, :].bitcast(f32),
                                        ALU.subtract).then_inc(w_lo_ready, 1)

            def split_state(count):
                for k in range(2):
                    dve.wait_ge(hT_hi_ready[k], count)
                    nc.vector.tensor_tensor(hT_lo[:, halves[k]], ps_hT[:, k, 0:HALF],
                                            hT_hi[:, halves[k]].bitcast(f32), ALU.subtract
                                            ).then_inc(hT_lo_ready[k], 1)

            for n in range(G * 2):
                split_piece(n, *pieces[n])
            split_state(1)
            for n in range(G * 2, 2 * G * 2):
                split_piece(n, *pieces[n])
            dve.wait_ge(bias_loaded, 32)
            nc.vector.tensor_tensor(bi[:, 0:2 * D], bi[:, 0:2 * D], bh[:, 0:2 * D], ALU.add).then_inc(bias_ready, 1)
            dve.wait_ge(bias_ready, 1)

            def columns(g):
                return slice(g * D, (g + 1) * D)

            def step(base, u, first_ring=False, more=True):
                t = base + u
                s, prev = u % 2, (u + 1) % 2
                add, mult, sub = ALU.add, ALU.mult, ALU.subtract
                tt = nc.vector.tensor_tensor
                dve.wait_ge(in_sum_ready, t + 1)
                tt(gin[:, :], ps_in[:, :], bi[:, columns(GATE_N)], add).then_inc(gin_ready, 1)
                dve.wait_ge(r_sum_ready, t + 1)
                tt(pre_r[:, :], ps_r[s][:, :], bi[:, columns(GATE_R)], add).then_inc(pre_r_ready, 1)
                dve.wait_ge(hn_sum_ready, t + 1)
                tt(ghn[:, :], ps_hn[:, :], bh[:, columns(GATE_N)], add).then_inc(ghn_ready, 1)
                dve.wait_ge(ghn_ready, t + 1)
                dve.wait_ge(r_ready, t + 1)
                tt(r_ghn[:, :], r_gate[:, :], ghn[:, :], mult).then_inc(r_ghn_ready, 1)
                dve.wait_ge(r_ghn_ready, t + 1)
                tt(pre_n[:, :], r_ghn[:, :], gin[:, :], add).then_inc(pre_n_ready, 1)
                dve.wait_ge(z_sum_ready, t + 1)
                tt(pre_z[:, :], ps_z[s][:, :], bi[:, columns(GATE_Z)], add).then_inc(pre_z_ready, 1)
                dve.wait_ge(n_ready, t + 1)
                tt(h_less_n[:, :], h[prev][:, :], n_gate[:, :], sub).then_inc(h_less_n_ready, 1)
                dve.wait_ge(h_less_n_ready, t + 1)
                dve.wait_ge(z_ready, t + 1)
                tt(z_part[:, :], z_gate[:, :], h_less_n[:, :], mult).then_inc(z_part_ready, 1)
                dve.wait_ge(z_part_ready, t + 1)
                tt(h[s][:, :], n_gate[:, :], z_part[:, :], add).then_inc(h_ready, 1)
                if more:
                    split_state(t + 2)
                else:
                    for k in range(2):
                        dve.wait_ge(hT_ready[k], t + 2)
                if not (first_ring and u < 2):
                    dve.wait_ge(out_stored[s], base * 8 + u // 2 * 16)
                tt(out_sb[s][:, :].rearrange("p (k n) -> p k n", k=2), ps_hT[:, :, 0:HALF],
                   x_raw[u][:, :].rearrange("p (k n) -> p k n", k=2), add).then_inc(out_ready, 1)

            for u in range(UNROLL):
                step(0, u, first_ring=True)
            with dve.Fori(1, TURNS - 1) as turn:
                for u in range(UNROLL):
                    step(turn * UNROLL, u)
            for u in range(UNROLL):
                step(LAST_BLOCK, u, more=u + 1 < UNROLL)


def kernel(**inputs):
    import numpy as np
    import concourse.bacc as bacc
    from concourse.bass_utils import run_bass_kernel_spmd

    x = np.ascontiguousarray(inputs["x"])
    B, T, D = x.shape
    C = D // P
    arrays = {
        "x_t": np.ascontiguousarray(x.transpose(1, 2, 0).reshape(T, C, P, B).transpose(0, 2, 1, 3)).reshape(T, P, C * B),
        "cond": np.ascontiguousarray(inputs["cond_2048"]),
        "w_ih": np.ascontiguousarray(inputs["L0_cond_W_ih"]),
        "w_hh": np.ascontiguousarray(inputs["L0_cond_W_hh"]),
        "b_ih": np.ascontiguousarray(inputs["L0_cond_b_ih"]),
        "b_hh": np.ascontiguousarray(inputs["L0_cond_b_hh"]),
    }
    nc = bacc.Bacc("TRN2", target_bir_lowering=False, num_devices=1)
    ins = [nc.dram_tensor(name, a.shape, mybir.dt.float32, kind="ExternalInput").ap() for name, a in arrays.items()]
    out = nc.dram_tensor("out_t", (T, P, C * B), mybir.dt.float32, kind="ExternalOutput").ap()
    build(nc, *ins, out)
    got = run_bass_kernel_spmd(nc, [arrays], core_ids=[0]).results[0]["out_t"]
    got = got.reshape(T, P, C, B).transpose(3, 0, 2, 1).reshape(B, T, D)
    return np.ascontiguousarray(got)
```

```python
from contextlib import ExitStack

import concourse.bass as bass
from concourse import mybir

P = 128
UNROLL = 4
GATE_R, GATE_Z, GATE_N = range(3)
STATE_ORDER = (GATE_R, GATE_N, GATE_Z)


def build(nc, x_t, cond, w_ih, w_hh, b_ih, b_hh, out_t):
    f32 = mybir.dt.float32
    f32r = mybir.dt.float32r
    ALU = mybir.AluOpType
    ACT = mybir.ActivationFunctionType

    T = x_t.shape[0]
    D = cond.shape[1]
    C = D // P
    G = w_ih.shape[1] // D
    HALF = D // 2
    HC = C // 2
    TURNS = T // UNROLL
    LAST_BLOCK = T - UNROLL
    assert T % UNROLL == 0 and TURNS >= 3 and cond.shape[0] == P

    with ExitStack() as ctx:
        def sb(name, shape, dt=f32):
            return ctx.enter_context(nc.sbuf_tensor(name, shape, dt))

        def bank(name):
            return ctx.enter_context(nc.psum_tensor(name, [P, D], f32))

        def sem(name):
            return ctx.enter_context(nc.semaphore(name))

        wi_raw = sb("wi_raw", [P, G, C, D])
        wi_hi = sb("wi_hi", [P, G, C, D], f32r)
        wi_lo = sb("wi_lo", [P, G, C, D], f32r)
        wh_raw = sb("wh_raw", [P, G, C, D])
        wh_hi = sb("wh_hi", [P, G, C, D], f32r)
        wh_lo = sb("wh_lo", [P, G, C, D], f32r)
        bi = sb("bi", [P, G * D])
        bh = sb("bh", [P, G * D])
        identity = sb("identity", [P, P])
        table_probe = sb("table_probe", [P, 2])
        x_raw = [sb(f"x_raw{s}", [P, D]) for s in range(UNROLL)]
        x_hi = [sb(f"x_hi{s}", [P, D], f32r) for s in range(2)]
        x_lo = [sb(f"x_lo{s}", [P, D], f32r) for s in range(2)]
        h = [sb(f"h{s}", [P, D]) for s in range(2)]
        hT_hi = sb("hT_hi", [P, D], f32r)
        hT_lo = sb("hT_lo", [P, D], f32r)
        gin = sb("gin", [P, D])
        scratch = sb("scratch", [P, 6, D])
        ghn, pre_r, pre_z, r_gate, z_gate, r_ghn = (scratch[:, n, :] for n in range(6))
        bias_rows = scratch[0:1, :, :].rearrange("p (m g) d -> p m (g d)", m=2)
        pre_n = sb("pre_n", [P, D])
        n_gate = sb("n_gate", [P, D])
        h_less_n = sb("h_less_n", [P, D])
        z_part = sb("z_part", [P, D])
        out_sb = [sb(f"out_sb{s}", [P, D]) for s in range(2)]

        ps_r = [bank(f"ps_r{s}") for s in range(2)]
        ps_z = [bank(f"ps_z{s}") for s in range(2)]
        ps_in = bank("ps_in")
        ps_hn = bank("ps_hn")
        ps_hT = ctx.enter_context(nc.psum_tensor("ps_hT", [P, 2, D], f32))

        pieces = [(False, GATE_R, c, c + 1) for c in range(C)]
        pieces += [(False, g, c, c + HC) for g in (GATE_Z, GATE_N) for c in (0, HC)]
        input_pieces = len(pieces)
        pieces += [(True, g, c, c + HC) for g in STATE_ORDER for c in (0, HC)]
        piece_of = {(hh, g, c): n for n, (hh, g, c0, c1) in enumerate(pieces) for c in range(c0, c1)}
        w_loaded = [sem(f"w_loaded{n}") for n in range(len(pieces))]
        bias_loaded = sem("bias_loaded")
        cond_loaded = sem("cond_loaded")
        x_loaded = [sem(f"x_loaded{s}") for s in range(UNROLL)]
        out_stored = [sem(f"out_stored{s}") for s in range(2)]
        identity_zeroed = sem("identity_zeroed")
        identity_ready = sem("identity_ready")
        bias_spread = sem("bias_spread")
        bias_ready = sem("bias_ready")
        probe_ready = sem("probe_ready")
        w_hi_ready = sem("w_hi_ready")
        w_lo_ready = sem("w_lo_ready")
        x_hi_ready = sem("x_hi_ready")
        x_lo_ready = sem("x_lo_ready")
        in_sum_ready = sem("in_sum_ready")
        r_sum_ready = sem("r_sum_ready")
        hn_sum_ready = sem("hn_sum_ready")
        z_sum_ready = sem("z_sum_ready")
        gin_ready = sem("gin_ready")
        pre_r_ready = sem("pre_r_ready")
        r_ready = sem("r_ready")
        ghn_ready = sem("ghn_ready")
        r_ghn_ready = sem("r_ghn_ready")
        pre_n_ready = sem("pre_n_ready")
        n_ready = sem("n_ready")
        pre_z_ready = sem("pre_z_ready")
        z_ready = sem("z_ready")
        h_less_n_ready = sem("h_less_n_ready")
        z_part_ready = sem("z_part_ready")
        h_ready = sem("h_ready")
        hT_ready = [sem(f"hT_ready{k}") for k in range(2)]
        hT_hi_ready = [sem(f"hT_hi_ready{k}") for k in range(2)]
        hT_lo_ready = [sem(f"hT_lo_ready{k}") for k in range(2)]
        out_ready = sem("out_ready")

        halves = [slice(0, HALF), slice(HALF, D)]
        w_raw, w_hi, w_lo = (wi_raw, wh_raw), (wi_hi, wh_hi), (wi_lo, wh_lo)

        def chunks_of(tensors, n):
            hh, g, c0, c1 = pieces[n]
            return tensors[hh][:, g, c0:c1, :]

        def columns(g):
            return slice(g * D, (g + 1) * D)

        block = ctx.enter_context(nc.Block())

        @block.sync
        def _(sp):
            def load_x(t, u):
                sp.dma_start(x_raw[u][:, :], x_t[bass.ds(t, 1), :, :].rearrange("a p n -> p (a n)")
                             ).then_inc(x_loaded[u], 16)

            def load_piece(n):
                hh, g, c0, c1 = pieces[n]
                rows = (w_ih, w_hh)[hh][c0 * P:c1 * P, g * D:(g + 1) * D]
                sp.dma_start(chunks_of(w_raw, n), rows.rearrange("(c p) n -> p c n", p=P)
                             ).then_inc(w_loaded[n], 16)

            for n in range(input_pieces):
                load_piece(n)
            sp.dma_start(h[1][:, :], cond[:, :]).then_inc(cond_loaded, 16)
            for n in range(input_pieces, len(pieces)):
                load_piece(n)
            for u in range(1, UNROLL):
                load_x(u, u)

            def step(t, u, more):
                sp.wait_ge(out_ready, t + 1)
                sp.dma_start(out_t[bass.ds(t, 1), :, :].rearrange("a p n -> p (a n)"), out_sb[u % 2][:, :]
                             ).then_inc(out_stored[u % 2], 16)
                if more:
                    load_x(t + UNROLL, u)

            for u in range(UNROLL):
                step(u, u, True)
            with sp.Fori(1, TURNS - 1) as turn:
                for u in range(UNROLL):
                    step(turn * UNROLL + u, u, True)
            for u in range(UNROLL):
                step(LAST_BLOCK + u, u, False)
            for s in range(2):
                sp.wait_ge(out_stored[s], 16 * (T // 2))

        @block.tensor
        def _(pe):
            def products(out, a_hi, a_lo, w_hi, w_lo, g, c, first, last):
                rows = slice(c * P, (c + 1) * P)
                nc.tensor.matmul(out[:, :], a_hi[:, rows], w_hi[:, g, c, :], start=first, stop=False)
                nc.tensor.matmul(out[:, :], a_hi[:, rows], w_lo[:, g, c, :], start=False, stop=False)
                return nc.tensor.matmul(out[:, :], a_lo[:, rows], w_hi[:, g, c, :], start=False, stop=last)

            def input_products(g, out, s, first_step):
                for c in range(C):
                    if first_step:
                        pe.wait_ge(w_lo_ready, piece_of[False, g, c] + 1)
                    last = products(out, x_hi[s], x_lo[s], wi_hi, wi_lo, g, c, c == 0, g == GATE_N and c == C - 1)
                return last

            def state_products(g, out, t, first_step):
                for c in range(C):
                    if g == STATE_ORDER[0] and c % HC == 0:
                        pe.wait_ge(hT_lo_ready[c // HC], t + 1)
                    if first_step:
                        pe.wait_ge(w_lo_ready, piece_of[True, g, c] + 1)
                    last = products(out, hT_hi, hT_lo, wh_hi, wh_lo, g, c, g == GATE_N and c == 0, c == C - 1)
                return last

            def transpose_state(s):
                for k in range(2):
                    for c in range(HC):
                        rows = slice((k * HC + c) * P, (k * HC + c + 1) * P)
                        last = nc.tensor.transpose(ps_hT[:, k, c * P:(c + 1) * P], h[s][:, rows], identity[:, :])
                    last.then_inc(hT_ready[k], 1)

            pe.wait_ge(x_hi_ready, 1)
            pe.wait_ge(x_lo_ready, 1)
            input_products(GATE_R, ps_r[0], 0, True)
            input_products(GATE_Z, ps_z[0], 0, True)
            pe.wait_ge(identity_ready, 1)
            pe.wait_ge(cond_loaded, 16)
            transpose_state(1)
            last = input_products(GATE_N, ps_in, 0, True)
            last.then_inc(in_sum_ready, 1)

            def step(t, u, first_step=False, more=True):
                s, nxt = u % 2, (u + 1) % 2
                for g in STATE_ORDER:
                    if g == GATE_N and not first_step:
                        pe.wait_ge(ghn_ready, t)
                    out, ready = {GATE_R: (ps_r[s], r_sum_ready), GATE_Z: (ps_z[s], z_sum_ready),
                                  GATE_N: (ps_hn, hn_sum_ready)}[g]
                    state_products(g, out, t, first_step).then_inc(ready, 1)
                if more:
                    pe.wait_ge(x_hi_ready, t + 2)
                    pe.wait_ge(x_lo_ready, t + 2)
                    if not first_step:
                        pe.wait_ge(pre_r_ready, t)
                        pe.wait_ge(pre_z_ready, t)
                    input_products(GATE_R, ps_r[nxt], nxt, False)
                    input_products(GATE_Z, ps_z[nxt], nxt, False)
                pe.wait_ge(h_ready, t + 1)
                if not first_step:
                    pe.wait_ge(out_ready, t)
                transpose_state(s)
                if more:
                    pe.wait_ge(gin_ready, t + 1)
                    input_products(GATE_N, ps_in, nxt, False).then_inc(in_sum_ready, 1)

            for u in range(UNROLL):
                step(u, u, first_step=u == 0)
            with pe.Fori(1, TURNS - 1) as turn:
                for u in range(UNROLL):
                    step(turn * UNROLL + u, u)
            for u in range(UNROLL):
                step(LAST_BLOCK + u, u, more=u < UNROLL - 1)

        @block.scalar
        def _(act):
            act.dma_start(x_raw[0][:, :], x_t[0, :, :]).then_inc(x_loaded[0], 16)
            act.wait_ge(probe_ready, 1)
            nc.scalar.activation(table_probe[:, 1:2], table_probe[:, 0:1], ACT.Sigmoid)
            for m, b in enumerate((b_ih, b_hh)):
                act.dma_start(bias_rows[:, m, :], b.rearrange("(a n) -> a n", a=1)).then_inc(bias_loaded, 16)

            def round_x(block_start, v):
                act.wait_ge(x_loaded[v], block_start * (16 // UNROLL) + 16)
                nc.scalar.activation(x_hi[v % 2][:, :], x_raw[v][:, :], ACT.Copy).then_inc(x_hi_ready, 1)

            def round_state(count):
                for k in range(2):
                    act.wait_ge(hT_ready[k], count)
                    nc.scalar.activation(hT_hi[:, halves[k]], ps_hT[:, k, 0:HALF], ACT.Copy
                                         ).then_inc(hT_hi_ready[k], 1)

            def round_piece(n):
                act.wait_ge(w_loaded[n], 16)
                nc.scalar.activation(chunks_of(w_hi, n), chunks_of(w_raw, n), ACT.Copy).then_inc(w_hi_ready, 1)

            round_x(0, 0)
            for n in range(input_pieces):
                round_piece(n)
            round_state(1)
            for n in range(input_pieces, len(pieces)):
                round_piece(n)
            round_x(0, 1)

            def step(base, u, more_x=True, more=True):
                t = base + u
                if more_x:
                    act.wait_ge(in_sum_ready, t + 1)
                    ahead = (u + 2) // UNROLL * UNROLL
                    round_x(base + ahead, u + 2 - ahead)
                act.wait_ge(pre_r_ready, t + 1)
                nc.scalar.activation(r_gate, pre_r, ACT.Sigmoid).then_inc(r_ready, 1)
                act.wait_ge(pre_n_ready, t + 1)
                nc.scalar.activation(n_gate[:, :], pre_n[:, :], ACT.Tanh).then_inc(n_ready, 1)
                act.wait_ge(pre_z_ready, t + 1)
                nc.scalar.activation(z_gate, pre_z, ACT.Sigmoid).then_inc(z_ready, 1)
                if more:
                    round_state(t + 2)

            for u in range(UNROLL):
                step(0, u)
            with act.Fori(1, TURNS - 1) as turn:
                for u in range(UNROLL):
                    step(turn * UNROLL, u)
            for u in range(UNROLL):
                step(LAST_BLOCK, u, more_x=u + 2 < UNROLL, more=u + 1 < UNROLL)

        @block.gpsimd
        def _(pool):
            nc.gpsimd.memset(identity[:, :], 0.0).then_inc(identity_zeroed, 1)
            pool.wait_ge(identity_zeroed, 1)
            nc.gpsimd.affine_select(out=identity[:, :], in_=identity[:, :], compare_op=ALU.not_equal, fill=1.0,
                                    base=0, pattern=[[-1, P]], channel_multiplier=1).then_inc(identity_ready, 1)

            def split_x(t, v):
                pool.wait_ge(x_hi_ready, t + 1)
                nc.gpsimd.tensor_tensor(x_lo[v % 2][:, :], x_raw[v][:, :], x_hi[v % 2][:, :].bitcast(f32),
                                        ALU.subtract).then_inc(x_lo_ready, 1)

            split_x(0, 0)
            pool.wait_ge(bias_loaded, 32)
            for m, b in enumerate((bi, bh)):
                nc.gpsimd.partition_broadcast(b[:, :], bias_rows[:, m, :]).then_inc(bias_spread, 1)
            pool.wait_ge(bias_spread, 2)
            nc.gpsimd.tensor_tensor(bi[:, 0:2 * D], bi[:, 0:2 * D], bh[:, 0:2 * D], ALU.add).then_inc(bias_ready, 1)
            for v in range(1, UNROLL):
                split_x(v, v)
            with pool.Fori(1, TURNS) as turn:
                for v in range(UNROLL):
                    split_x(turn * UNROLL + v, v)

        @block.vector
        def _(dve):
            def split_piece(n):
                dve.wait_ge(w_hi_ready, n + 1)
                nc.vector.tensor_tensor(chunks_of(w_lo, n), chunks_of(w_raw, n), chunks_of(w_hi, n).bitcast(f32),
                                        ALU.subtract).then_inc(w_lo_ready, 1)

            def split_state(count):
                for k in range(2):
                    dve.wait_ge(hT_hi_ready[k], count)
                    nc.vector.tensor_tensor(hT_lo[:, halves[k]], ps_hT[:, k, 0:HALF],
                                            hT_hi[:, halves[k]].bitcast(f32), ALU.subtract
                                            ).then_inc(hT_lo_ready[k], 1)

            nc.vector.memset(table_probe[:, 0:1], 0.0).then_inc(probe_ready, 1)
            for n in range(input_pieces):
                split_piece(n)
            split_state(1)
            for n in range(input_pieces, len(pieces)):
                split_piece(n)
            dve.wait_ge(bias_ready, 1)

            def step(base, u, first_ring=False, more=True):
                t = base + u
                s, prev = u % 2, (u + 1) % 2
                add, mult, sub = ALU.add, ALU.mult, ALU.subtract
                tt = nc.vector.tensor_tensor
                dve.wait_ge(in_sum_ready, t + 1)
                tt(gin[:, :], ps_in[:, :], bi[:, columns(GATE_N)], add).then_inc(gin_ready, 1)
                dve.wait_ge(r_sum_ready, t + 1)
                tt(pre_r, ps_r[s][:, :], bi[:, columns(GATE_R)], add).then_inc(pre_r_ready, 1)
                dve.wait_ge(hn_sum_ready, t + 1)
                tt(ghn, ps_hn[:, :], bh[:, columns(GATE_N)], add).then_inc(ghn_ready, 1)
                dve.wait_ge(ghn_ready, t + 1)
                dve.wait_ge(r_ready, t + 1)
                tt(r_ghn, r_gate, ghn, mult).then_inc(r_ghn_ready, 1)
                dve.wait_ge(r_ghn_ready, t + 1)
                tt(pre_n[:, :], r_ghn, gin[:, :], add).then_inc(pre_n_ready, 1)
                dve.wait_ge(z_sum_ready, t + 1)
                tt(pre_z, ps_z[s][:, :], bi[:, columns(GATE_Z)], add).then_inc(pre_z_ready, 1)
                dve.wait_ge(n_ready, t + 1)
                tt(h_less_n[:, :], h[prev][:, :], n_gate[:, :], sub).then_inc(h_less_n_ready, 1)
                dve.wait_ge(h_less_n_ready, t + 1)
                dve.wait_ge(z_ready, t + 1)
                tt(z_part[:, :], z_gate, h_less_n[:, :], mult).then_inc(z_part_ready, 1)
                dve.wait_ge(z_part_ready, t + 1)
                tt(h[s][:, :], n_gate[:, :], z_part[:, :], add).then_inc(h_ready, 1)
                if more:
                    split_state(t + 2)
                else:
                    for k in range(2):
                        dve.wait_ge(hT_ready[k], t + 2)
                if not (first_ring and u < 2):
                    dve.wait_ge(out_stored[s], base * 8 + u // 2 * 16)
                tt(out_sb[s][:, :].rearrange("p (k n) -> p k n", k=2), ps_hT[:, :, 0:HALF],
                   x_raw[u][:, :].rearrange("p (k n) -> p k n", k=2), add).then_inc(out_ready, 1)

            for u in range(UNROLL):
                step(0, u, first_ring=True)
            with dve.Fori(1, TURNS - 1) as turn:
                for u in range(UNROLL):
                    step(turn * UNROLL, u)
            for u in range(UNROLL):
                step(LAST_BLOCK, u, more=u + 1 < UNROLL)


def kernel(**inputs):
    import numpy as np
    import concourse.bacc as bacc
    from concourse.bass_utils import run_bass_kernel_spmd

    x = np.ascontiguousarray(inputs["x"])
    B, T, D = x.shape
    C = D // P
    arrays = {
        "x_t": np.ascontiguousarray(x.transpose(1, 2, 0).reshape(T, C, P, B).transpose(0, 2, 1, 3)).reshape(T, P, C * B),
        "cond": np.ascontiguousarray(inputs["cond_2048"]),
        "w_ih": np.ascontiguousarray(inputs["L0_cond_W_ih"]),
        "w_hh": np.ascontiguousarray(inputs["L0_cond_W_hh"]),
        "b_ih": np.ascontiguousarray(inputs["L0_cond_b_ih"]),
        "b_hh": np.ascontiguousarray(inputs["L0_cond_b_hh"]),
    }
    nc = bacc.Bacc("TRN2", target_bir_lowering=False, num_devices=1)
    ins = [nc.dram_tensor(name, a.shape, mybir.dt.float32, kind="ExternalInput").ap() for name, a in arrays.items()]
    out = nc.dram_tensor("out_t", (T, P, C * B), mybir.dt.float32, kind="ExternalOutput").ap()
    build(nc, *ins, out)
    got = run_bass_kernel_spmd(nc, [arrays], core_ids=[0]).results[0]["out_t"]
    got = got.reshape(T, P, C, B).transpose(3, 0, 2, 1).reshape(B, T, D)
    return np.ascontiguousarray(got)
```

```python
from contextlib import ExitStack

import concourse.bass as bass
from concourse import mybir

P = 128
UNROLL = 4
B = 32
VECTOR_MOVES = 9
GATE_R, GATE_Z, GATE_N = range(3)
STATE_ORDER = (GATE_R, GATE_N, GATE_Z)


def build(nc, x_t, x_last, cond, cond_t, w_ih, w_hh, b_ih, b_hh, out_t):
    f32 = mybir.dt.float32
    f32r = mybir.dt.float32r
    ALU = mybir.AluOpType
    ACT = mybir.ActivationFunctionType

    T = x_t.shape[0]
    D = cond.shape[1]
    C = D // P
    G = w_ih.shape[1] // D
    HALF = D // 2
    HC = C // 2
    TURNS = T // UNROLL
    LAST_BLOCK = T - UNROLL
    assert T % UNROLL == 0 and TURNS >= 3 and cond.shape[0] == P

    with ExitStack() as ctx:
        def sb(name, shape, dt=f32):
            return ctx.enter_context(nc.sbuf_tensor(name, shape, dt))

        def bank(name):
            return ctx.enter_context(nc.psum_tensor(name, [P, D], f32))

        def sem(name):
            return ctx.enter_context(nc.semaphore(name))

        wi_raw = sb("wi_raw", [P, G, C, D])
        wi_hi = sb("wi_hi", [P, G, C, D], f32r)
        wi_lo = sb("wi_lo", [P, G, C, D], f32r)
        wh_raw = sb("wh_raw", [P, G, C, D])
        wh_hi = sb("wh_hi", [P, G, C, D], f32r)
        wh_lo = sb("wh_lo", [P, G, C, D], f32r)
        bi = sb("bi", [P, G * D])
        bh = sb("bh", [P, G * D])
        table_probe = sb("table_probe", [P, 2])
        x_raw = [sb(f"x_raw{s}", [P, D]) for s in range(UNROLL)]
        x_hi = [sb(f"x_hi{s}", [P, D], f32r) for s in range(2)]
        x_lo = [sb(f"x_lo{s}", [P, D], f32r) for s in range(2)]
        h = [sb(f"h{s}", [P, D]) for s in range(2)]
        hT_blocks = sb("hT_blocks", [P, D])
        hT = sb("hT", [P, D])
        hT_hi = sb("hT_hi", [P, D], f32r)
        hT_lo = sb("hT_lo", [P, D], f32r)
        gin = sb("gin", [P, D])
        scratch = sb("scratch", [P, 6, D])
        ghn, pre_r, pre_z, r_gate, z_gate, r_ghn = (scratch[:, n, :] for n in range(6))
        bias_rows = scratch[0:1, :, :].rearrange("p (m g) d -> p m (g d)", m=2)
        n_gate = sb("n_gate", [P, D])
        h_less_n = sb("h_less_n", [P, D])
        out_sb = [sb(f"out_sb{s}", [P, D]) for s in range(2)]

        ps_r = [bank(f"ps_r{s}") for s in range(2)]
        ps_z = [bank(f"ps_z{s}") for s in range(2)]
        ps_in = bank("ps_in")
        ps_hn = bank("ps_hn")

        pieces = [(False, GATE_R, c, c + 1) for c in range(C)]
        pieces += [(False, g, c, c + HC) for g in (GATE_Z, GATE_N) for c in (0, HC)]
        input_pieces = len(pieces)
        pieces += [(True, g, c, c + HC) for g in STATE_ORDER[:-1] for c in (0, HC)]
        pieces += [(True, STATE_ORDER[-1], c, c + 1) for c in range(C)]
        piece_of = {(hh, g, c): n for n, (hh, g, c0, c1) in enumerate(pieces) for c in range(c0, c1)}
        w_loaded = [sem(f"w_loaded{n}") for n in range(len(pieces))]
        bias_loaded = sem("bias_loaded")
        cond_loaded = sem("cond_loaded")
        cond_t_loaded = sem("cond_t_loaded")
        x_last_loaded = sem("x_last_loaded")
        x_loaded = [sem(f"x_loaded{s}") for s in range(UNROLL)]
        out_stored = [sem(f"out_stored{s}") for s in range(2)]
        bias_spread = sem("bias_spread")
        bias_ready = sem("bias_ready")
        probe_ready = sem("probe_ready")
        w_hi_ready = sem("w_hi_ready")
        w_lo_ready = sem("w_lo_ready")
        x_hi_ready = sem("x_hi_ready")
        x_lo_ready = sem("x_lo_ready")
        in_sum_ready = sem("in_sum_ready")
        r_sum_ready = sem("r_sum_ready")
        hn_sum_ready = sem("hn_sum_ready")
        z_sum_ready = sem("z_sum_ready")
        gin_ready = sem("gin_ready")
        pre_r_ready = sem("pre_r_ready")
        r_ready = sem("r_ready")
        ghn_ready = sem("ghn_ready")
        r_ghn_ready = sem("r_ghn_ready")
        pre_n_ready = sem("pre_n_ready")
        n_ready = sem("n_ready")
        pre_z_ready = sem("pre_z_ready")
        z_ready = sem("z_ready")
        h_less_n_ready = sem("h_less_n_ready")
        z_part_ready = sem("z_part_ready")
        h_ready = sem("h_ready")
        blocks_ready = sem("blocks_ready")
        moved_by_vector = sem("moved_by_vector")
        moved_by_scalar = sem("moved_by_scalar")
        hT_hi_ready = [sem(f"hT_hi_ready{k}") for k in range(2)]
        hT_lo_ready = [sem(f"hT_lo_ready{k}") for k in range(2)]
        out_ready = sem("out_ready")

        halves = [slice(0, HALF), slice(HALF, D)]
        w_raw, w_hi, w_lo = (wi_raw, wh_raw), (wi_hi, wh_hi), (wi_lo, wh_lo)

        moves = [(q, a) for q in range(P // B) for a in range(P // B)]

        def block_move(q, a):
            to = hT[a * B:(a + 1) * B, :].rearrange("p (c n) -> p c n", c=C)[:, :, q * B:(q + 1) * B]
            return to, hT_blocks[q * B:(q + 1) * B, :].rearrange("p (c n) -> p c n", c=C)[:, :, a * B:(a + 1) * B]

        def chunks_of(tensors, n):
            hh, g, c0, c1 = pieces[n]
            return tensors[hh][:, g, c0:c1, :]

        def columns(g):
            return slice(g * D, (g + 1) * D)

        block = ctx.enter_context(nc.Block())

        @block.sync
        def _(sp):
            def load_x(t, u):
                sp.dma_start(x_raw[u][:, :], x_t[bass.ds(t, 1), :, :].rearrange("a p n -> p (a n)")
                             ).then_inc(x_loaded[u], 16)

            def load_piece(n):
                hh, g, c0, c1 = pieces[n]
                rows = (w_ih, w_hh)[hh][c0 * P:c1 * P, g * D:(g + 1) * D]
                sp.dma_start(chunks_of(w_raw, n), rows.rearrange("(c p) n -> p c n", p=P)
                             ).then_inc(w_loaded[n], 16)

            for n in range(input_pieces):
                load_piece(n)
            sp.dma_start(hT[:, :], cond_t[:, :]).then_inc(cond_t_loaded, 16)
            for n in range(input_pieces, len(pieces)):
                load_piece(n)
            sp.dma_start(h[1][:, :], cond[:, :]).then_inc(cond_loaded, 16)
            for u in range(1, UNROLL):
                load_x(u, u)

            def step(t, u, more):
                sp.wait_ge(out_ready, t + 1)
                sp.dma_start(out_t[bass.ds(t, 1), :, :].rearrange("a p n -> p (a n)"), out_sb[u % 2][:, :]
                             ).then_inc(out_stored[u % 2], 16)
                if more:
                    load_x(t + UNROLL, u)

            for u in range(UNROLL):
                step(u, u, True)
            with sp.Fori(1, TURNS - 1) as turn:
                for u in range(UNROLL):
                    step(turn * UNROLL + u, u, True)
            for u in range(UNROLL - 1):
                step(LAST_BLOCK + u, u, False)
                if u == 0:
                    sp.dma_start(x_raw[0][:, :], x_last[:, :]).then_inc(x_last_loaded, 16)
            for k in range(2):
                sp.wait_ge(out_ready, T + k)
                sp.dma_start(out_t[T - 1, :, halves[k]], out_sb[1][:, halves[k]]).then_inc(out_stored[1], 16)
            sp.wait_ge(out_stored[0], 16 * (T // 2))
            sp.wait_ge(out_stored[1], 16 * (T // 2 + 1))

        @block.tensor
        def _(pe):
            def products(out, a_hi, a_lo, w_hi, w_lo, g, c, first, last):
                rows = slice(c * P, (c + 1) * P)
                nc.tensor.matmul(out[:, :], a_hi[:, rows], w_hi[:, g, c, :], start=first, stop=False)
                nc.tensor.matmul(out[:, :], a_hi[:, rows], w_lo[:, g, c, :], start=False, stop=False)
                return nc.tensor.matmul(out[:, :], a_lo[:, rows], w_hi[:, g, c, :], start=False, stop=last)

            def input_products(g, out, s, first_step):
                for c in range(C):
                    if first_step:
                        pe.wait_ge(w_lo_ready, piece_of[False, g, c] + 1)
                    last = products(out, x_hi[s], x_lo[s], wi_hi, wi_lo, g, c, c == 0, g == GATE_N and c == C - 1)
                return last

            def state_products(g, out, t, first_step):
                for c in range(C):
                    if g == STATE_ORDER[0] and c % HC == 0:
                        pe.wait_ge(hT_lo_ready[c // HC], t + 1)
                    if first_step:
                        pe.wait_ge(w_lo_ready, piece_of[True, g, c] + 1)
                    last = products(out, hT_hi, hT_lo, wh_hi, wh_lo, g, c, g == GATE_N and c == 0, c == C - 1)
                return last

            pe.wait_ge(x_hi_ready, 1)
            pe.wait_ge(x_lo_ready, 1)
            input_products(GATE_R, ps_r[0], 0, True)
            input_products(GATE_Z, ps_z[0], 0, True)
            last = input_products(GATE_N, ps_in, 0, True)
            last.then_inc(in_sum_ready, 1)

            def step(t, u, first_step=False, more=True):
                s, nxt = u % 2, (u + 1) % 2
                for g in STATE_ORDER:
                    if g == GATE_N and not first_step:
                        pe.wait_ge(ghn_ready, t)
                    out, ready = {GATE_R: (ps_r[s], r_sum_ready), GATE_Z: (ps_z[s], z_sum_ready),
                                  GATE_N: (ps_hn, hn_sum_ready)}[g]
                    state_products(g, out, t, first_step).then_inc(ready, 1)
                if more:
                    pe.wait_ge(x_hi_ready, t + 2)
                    pe.wait_ge(x_lo_ready, t + 2)
                    if not first_step:
                        pe.wait_ge(pre_r_ready, t)
                        pe.wait_ge(pre_z_ready, t)
                    input_products(GATE_R, ps_r[nxt], nxt, False)
                    input_products(GATE_Z, ps_z[nxt], nxt, False)
                    pe.wait_ge(gin_ready, t + 1)
                    input_products(GATE_N, ps_in, nxt, False).then_inc(in_sum_ready, 1)

            for u in range(UNROLL):
                step(u, u, first_step=u == 0)
            with pe.Fori(1, TURNS - 1) as turn:
                for u in range(UNROLL):
                    step(turn * UNROLL + u, u)
            for u in range(UNROLL):
                step(LAST_BLOCK + u, u, more=u < UNROLL - 1)

        @block.scalar
        def _(act):
            act.dma_start(x_raw[0][:, :], x_t[0, :, :]).then_inc(x_loaded[0], 16)
            act.wait_ge(probe_ready, 1)
            nc.scalar.activation(table_probe[:, 1:2], table_probe[:, 0:1], ACT.Sigmoid)
            for m, b in enumerate((b_ih, b_hh)):
                act.dma_start(bias_rows[:, m, :], b.rearrange("(a n) -> a n", a=1)).then_inc(bias_loaded, 16)

            def round_x(block_start, v):
                act.wait_ge(x_loaded[v], block_start * (16 // UNROLL) + 16)
                nc.scalar.activation(x_hi[v % 2][:, :], x_raw[v][:, :], ACT.Copy).then_inc(x_hi_ready, 1)

            def move_blocks(t, first_step):
                act.wait_ge(blocks_ready, t + 1)
                if not first_step:
                    act.wait_ge(out_ready, t)
                for q, a in moves[VECTOR_MOVES:]:
                    to, what = block_move(q, a)
                    last = nc.scalar.activation(to, what, ACT.Copy)
                last.then_inc(moved_by_scalar, 1)

            def round_state():
                for k in range(2):
                    nc.scalar.activation(hT_hi[:, halves[k]], hT[:, halves[k]], ACT.Copy
                                         ).then_inc(hT_hi_ready[k], 1)

            def round_piece(n):
                act.wait_ge(w_loaded[n], 16)
                nc.scalar.activation(chunks_of(w_hi, n), chunks_of(w_raw, n), ACT.Copy).then_inc(w_hi_ready, 1)

            round_x(0, 0)
            for n in range(input_pieces):
                round_piece(n)
            act.wait_ge(cond_t_loaded, 16)
            round_state()
            for n in range(input_pieces, len(pieces)):
                round_piece(n)
            round_x(0, 1)

            def step(base, u, first_step=False, more_x=True):
                t = base + u
                if more_x:
                    act.wait_ge(in_sum_ready, t + 1)
                    ahead = (u + 2) // UNROLL * UNROLL
                    round_x(base + ahead, u + 2 - ahead)
                act.wait_ge(pre_r_ready, t + 1)
                nc.scalar.activation(r_gate, pre_r, ACT.Sigmoid).then_inc(r_ready, 1)
                act.wait_ge(pre_n_ready, t + 1)
                nc.scalar.activation(n_gate[:, :], n_gate[:, :], ACT.Tanh).then_inc(n_ready, 1)
                act.wait_ge(pre_z_ready, t + 1)
                nc.scalar.activation(z_gate, pre_z, ACT.Sigmoid).then_inc(z_ready, 1)
                move_blocks(t, first_step)
                act.wait_ge(moved_by_vector, t + 1)
                act.wait_ge(moved_by_scalar, t + 1)
                round_state()

            for u in range(UNROLL):
                step(0, u, first_step=u == 0)
            with act.Fori(1, TURNS - 1) as turn:
                for u in range(UNROLL):
                    step(turn * UNROLL, u)
            for u in range(UNROLL - 1):
                step(LAST_BLOCK, u, more_x=u + 2 < UNROLL)
            act.wait_ge(pre_r_ready, T)
            nc.scalar.activation(r_gate, pre_r, ACT.Sigmoid).then_inc(r_ready, 1)
            act.wait_ge(pre_n_ready, T)
            nc.scalar.activation(n_gate[:, :], n_gate[:, :], ACT.Tanh).then_inc(n_ready, 1)
            for k in range(2):
                act.wait_ge(pre_z_ready, T + k)
                nc.scalar.activation(z_gate[:, halves[k]], pre_z[:, halves[k]], ACT.Sigmoid).then_inc(z_ready, 1)

        @block.gpsimd
        def _(pool):
            def split_x(t, v):
                pool.wait_ge(x_hi_ready, t + 1)
                nc.gpsimd.tensor_tensor(x_lo[v % 2][:, :], x_raw[v][:, :], x_hi[v % 2][:, :].bitcast(f32),
                                        ALU.subtract).then_inc(x_lo_ready, 1)

            split_x(0, 0)
            pool.wait_ge(bias_loaded, 32)
            for m, b in enumerate((bi, bh)):
                nc.gpsimd.partition_broadcast(b[:, :], bias_rows[:, m, :]).then_inc(bias_spread, 1)
            pool.wait_ge(bias_spread, 2)
            nc.gpsimd.tensor_tensor(bi[:, 0:2 * D], bi[:, 0:2 * D], bh[:, 0:2 * D], ALU.add).then_inc(bias_ready, 1)
            for v in range(1, UNROLL):
                split_x(v, v)
            with pool.Fori(1, TURNS) as turn:
                for v in range(UNROLL):
                    split_x(turn * UNROLL + v, v)

        @block.vector
        def _(dve):
            def split_piece(n):
                dve.wait_ge(w_hi_ready, n + 1)
                nc.vector.tensor_tensor(chunks_of(w_lo, n), chunks_of(w_raw, n), chunks_of(w_hi, n).bitcast(f32),
                                        ALU.subtract).then_inc(w_lo_ready, 1)

            def transpose_state(t, s, first_step):
                dve.wait_ge(h_ready, t + 1)
                nc.vector.transpose(hT_blocks[:, :], h[s][:, :]).then_inc(blocks_ready, 1)
                dve.wait_ge(blocks_ready, t + 1)
                if first_step:
                    dve.wait_ge(hT_lo_ready[1], 1)
                else:
                    dve.wait_ge(out_ready, t)
                for q, a in moves[:VECTOR_MOVES]:
                    to, what = block_move(q, a)
                    last = nc.vector.tensor_copy(to, what)
                last.then_inc(moved_by_vector, 1)

            def split_state(count):
                for k in range(2):
                    dve.wait_ge(hT_hi_ready[k], count)
                    nc.vector.tensor_tensor(hT_lo[:, halves[k]], hT[:, halves[k]],
                                            hT_hi[:, halves[k]].bitcast(f32), ALU.subtract
                                            ).then_inc(hT_lo_ready[k], 1)

            nc.vector.memset(table_probe[:, 0:1], 0.0).then_inc(probe_ready, 1)
            for n in range(input_pieces):
                split_piece(n)
            split_state(1)
            for n in range(input_pieces, len(pieces)):
                split_piece(n)
            dve.wait_ge(bias_ready, 1)
            dve.wait_ge(cond_loaded, 16)

            add, mult, sub = ALU.add, ALU.mult, ALU.subtract
            tt = nc.vector.tensor_tensor

            def reset_and_new(t, s):
                dve.wait_ge(in_sum_ready, t + 1)
                tt(gin[:, :], ps_in[:, :], bi[:, columns(GATE_N)], add).then_inc(gin_ready, 1)
                dve.wait_ge(r_sum_ready, t + 1)
                tt(pre_r, ps_r[s][:, :], bi[:, columns(GATE_R)], add).then_inc(pre_r_ready, 1)
                dve.wait_ge(hn_sum_ready, t + 1)
                tt(ghn, ps_hn[:, :], bh[:, columns(GATE_N)], add).then_inc(ghn_ready, 1)
                dve.wait_ge(ghn_ready, t + 1)
                dve.wait_ge(r_ready, t + 1)
                tt(r_ghn, r_gate, ghn, mult).then_inc(r_ghn_ready, 1)
                dve.wait_ge(r_ghn_ready, t + 1)
                tt(n_gate[:, :], r_ghn, gin[:, :], add).then_inc(pre_n_ready, 1)

            def step(base, u, first_ring=False):
                t = base + u
                s, prev = u % 2, (u + 1) % 2
                reset_and_new(t, s)
                dve.wait_ge(z_sum_ready, t + 1)
                tt(pre_z, ps_z[s][:, :], bi[:, columns(GATE_Z)], add).then_inc(pre_z_ready, 1)
                dve.wait_ge(n_ready, t + 1)
                tt(h_less_n[:, :], h[prev][:, :], n_gate[:, :], sub).then_inc(h_less_n_ready, 1)
                dve.wait_ge(h_less_n_ready, t + 1)
                dve.wait_ge(z_ready, t + 1)
                tt(h_less_n[:, :], z_gate, h_less_n[:, :], mult).then_inc(z_part_ready, 1)
                dve.wait_ge(z_part_ready, t + 1)
                tt(h[s][:, :], n_gate[:, :], h_less_n[:, :], add).then_inc(h_ready, 1)
                transpose_state(t, s, first_ring and u == 0)
                split_state(t + 2)
                dve.wait_ge(moved_by_vector, t + 1)
                dve.wait_ge(moved_by_scalar, t + 1)
                if not (first_ring and u < 2):
                    dve.wait_ge(out_stored[s], base * 8 + u // 2 * 16)
                tt(out_sb[s][:, :], hT[:, :], x_raw[u][:, :], add).then_inc(out_ready, 1)

            def last_step():
                reset_and_new(T - 1, 1)
                dve.wait_ge(z_sum_ready, T)
                for k in range(2):
                    z_bias = bi[:, GATE_Z * D + k * HALF:GATE_Z * D + (k + 1) * HALF]
                    tt(pre_z[:, halves[k]], ps_z[1][:, halves[k]], z_bias, add).then_inc(pre_z_ready, 1)
                dve.wait_ge(n_ready, T)
                tt(h_less_n[:, :], h[0][:, :], n_gate[:, :], sub).then_inc(h_less_n_ready, 1)
                dve.wait_ge(h_less_n_ready, T)
                dve.wait_ge(x_last_loaded, 16)
                dve.wait_ge(out_stored[1], 16 * (T // 2 - 1))
                for k, cols in enumerate(halves):
                    dve.wait_ge(z_ready, T + k)
                    tt(h_less_n[:, cols], z_gate[:, cols], h_less_n[:, cols], mult).then_inc(z_part_ready, 1)
                for k, cols in enumerate(halves):
                    dve.wait_ge(z_part_ready, T + k)
                    tt(h[1][:, cols], n_gate[:, cols], h_less_n[:, cols], add).then_inc(h_ready, 1)
                for k, cols in enumerate(halves):
                    dve.wait_ge(h_ready, T + k)
                    tt(out_sb[1][:, cols], h[1][:, cols], x_raw[0][:, cols], add).then_inc(out_ready, 1)

            for u in range(UNROLL):
                step(0, u, first_ring=True)
            with dve.Fori(1, TURNS - 1) as turn:
                for u in range(UNROLL):
                    step(turn * UNROLL, u)
            for u in range(UNROLL - 1):
                step(LAST_BLOCK, u)
            last_step()


def kernel(**inputs):
    import numpy as np
    import concourse.bacc as bacc
    from concourse.bass_utils import run_bass_kernel_spmd

    x = np.ascontiguousarray(inputs["x"])
    batch, T, D = x.shape
    C = D // P
    x_t = x.transpose(1, 2, 0).reshape(T, C, P, batch).transpose(0, 2, 1, 3)
    cond = np.ascontiguousarray(inputs["cond_2048"])
    arrays = {
        "x_t": np.ascontiguousarray(x_t).reshape(T, P, C * batch),
        "x_last": np.ascontiguousarray(x[:, T - 1]),
        "cond": cond,
        "cond_t": np.ascontiguousarray(cond.T.reshape(C, P, batch).transpose(1, 0, 2)).reshape(P, C * batch),
        "w_ih": np.ascontiguousarray(inputs["L0_cond_W_ih"]),
        "w_hh": np.ascontiguousarray(inputs["L0_cond_W_hh"]),
        "b_ih": np.ascontiguousarray(inputs["L0_cond_b_ih"]),
        "b_hh": np.ascontiguousarray(inputs["L0_cond_b_hh"]),
    }
    nc = bacc.Bacc("TRN2", target_bir_lowering=False, num_devices=1)
    ins = [nc.dram_tensor(name, a.shape, mybir.dt.float32, kind="ExternalInput").ap() for name, a in arrays.items()]
    out = nc.dram_tensor("out_t", (T, P, C * batch), mybir.dt.float32, kind="ExternalOutput").ap()
    build(nc, *ins, out)
    got = run_bass_kernel_spmd(nc, [arrays], core_ids=[0]).results[0]["out_t"]
    out = got.reshape(T, P, C, batch).transpose(3, 0, 2, 1).reshape(batch, T, D).copy()
    out[:, T - 1] = got[T - 1]
    return out
```
